# Optimizing a Trainium2 kernel written in Bass

```python
import numpy as np
import jax
import jax.numpy as jnp

def _softmax(x, axis=-1):
    return jax.nn.softmax(x, axis=axis)

def _gelu(x):
    return jax.nn.gelu(x, approximate=True)

def _silu(x):
    return jax.nn.silu(x)

def _sigmoid(x):
    return jax.nn.sigmoid(x)

def _layernorm(x, axis=-1, eps=1e-05):
    m = jnp.mean(x, axis=axis, keepdims=True)
    v = jnp.var(x, axis=axis, keepdims=True)
    return (x - m) / jnp.sqrt(v + eps)

def _scatter_add(tgt, idx, src, axis=0):
    return tgt.at[idx].add(src)

def _segment_sum(src, seg, n):
    return jax.ops.segment_sum(src, seg, n)
kernel_name = 'mk_adj_resnorm_d1_adj_r2_a04717'

def setup_inputs(seed: int=0):
    np.random.seed(seed)
    _w = jnp.asarray

    def _rec_inputs():
        import jax
        import jax.numpy as jnp
        _gk = jax.random.key(seed)
        x = -0.0005207 + 1.001 * jax.random.normal(jax.random.fold_in(_gk, 1), (8192, 128), jnp.float32)
        _w = (1.0 + jnp.arange(8192, dtype=jnp.float32)) ** (-0.5)
        _w = _w / _w.mean()
        _pij = jnp.clip(0.000244141 * _w[:, None] * _w[None, :], 0.0, 1.0)
        _a = jax.random.uniform(jax.random.fold_in(_gk, 2), (8192, 8192)) < _pij
        _a = jnp.logical_or(_a, jnp.eye(8192, dtype=bool))
        _af = _a.astype(jnp.float32)
        _af = _af * jax.random.uniform(jax.random.fold_in(_gk, 3), (8192, 8192), jnp.float32, 0.05, 1)
        adj = _af
        return (x, adj)
    x, adj = _rec_inputs()

    def _L0_gnn_setup():
        import jax, jax.numpy as jnp
        import numpy as np
        N, DIM = (8192, 128)

        def _gru_cell(x, h, W_ih, W_hh, b_ih, b_hh):
            gi = x @ W_ih.T + b_ih
            gh = h @ W_hh.T + b_hh
            i_r, i_z, i_n = jnp.split(gi, 3, axis=-1)
            h_r, h_z, h_n = jnp.split(gh, 3, axis=-1)
            r = jax.nn.sigmoid(i_r + h_r)
            z = jax.nn.sigmoid(i_z + h_z)
            n = jnp.tanh(i_n + r * h_n)
            return (1.0 - z) * n + z * h
        key = jax.random.key(seed)
        ks = jax.random.split(key, 8)
        states = jax.random.normal(ks[0], (N, DIM), dtype=jnp.float32)
        adj = jax.random.uniform(ks[1], (N, N), dtype=jnp.float32)
        s = 1.0 / np.sqrt(DIM)
        W_msg = jax.random.uniform(ks[2], (DIM, DIM), minval=-s, maxval=s, dtype=jnp.float32)
        b_msg = jax.random.uniform(ks[3], (DIM,), minval=-s, maxval=s, dtype=jnp.float32)
        W_ih = jax.random.uniform(ks[4], (3 * DIM, DIM), minval=-s, maxval=s, dtype=jnp.float32)
        W_hh = jax.random.uniform(ks[5], (3 * DIM, DIM), minval=-s, maxval=s, dtype=jnp.float32)
        b_ih = jax.random.uniform(ks[6], (3 * DIM,), minval=-s, maxval=s, dtype=jnp.float32)
        b_hh = jax.random.uniform(ks[7], (3 * DIM,), minval=-s, maxval=s, dtype=jnp.float32)
        return {'states': states, 'adj': adj, 'W_msg': W_msg, 'b_msg': b_msg, 'W_ih': W_ih, 'W_hh': W_hh, 'b_ih': b_ih, 'b_hh': b_hh}
    _L0_gnn_all = _L0_gnn_setup()
    _L0_gnn_in = {k: v for k, v in _L0_gnn_all.items() if k in ('W_msg', 'b_msg', 'W_ih', 'W_hh', 'b_ih', 'b_hh')}
    del _L0_gnn_all
    return {'x': x, 'adj': adj, 'L0_gnn_W_msg': _L0_gnn_in['W_msg'], 'L0_gnn_b_msg': _L0_gnn_in['b_msg'], 'L0_gnn_W_ih': _L0_gnn_in['W_ih'], 'L0_gnn_W_hh': _L0_gnn_in['W_hh'], 'L0_gnn_b_ih': _L0_gnn_in['b_ih'], 'L0_gnn_b_hh': _L0_gnn_in['b_hh']}

def reference(x, adj, L0_gnn_W_msg, L0_gnn_b_msg, L0_gnn_W_ih, L0_gnn_W_hh, L0_gnn_b_ih, L0_gnn_b_hh):
    import jax
    import jax.numpy as jnp

    def _L0_gnn_ref(states, adj, W_msg, b_msg, W_ih, W_hh, b_ih, b_hh):
        import jax, jax.numpy as jnp
        import numpy as np
        N, DIM = (8192, 128)

        def _gru_cell(x, h, W_ih, W_hh, b_ih, b_hh):
            gi = x @ W_ih.T + b_ih
            gh = h @ W_hh.T + b_hh
            i_r, i_z, i_n = jnp.split(gi, 3, axis=-1)
            h_r, h_z, h_n = jnp.split(gh, 3, axis=-1)
            r = jax.nn.sigmoid(i_r + h_r)
            z = jax.nn.sigmoid(i_z + h_z)
            n = jnp.tanh(i_n + r * h_n)
            return (1.0 - z) * n + z * h
        agg = adj @ states
        msg = jax.nn.relu(agg @ W_msg.T + b_msg)
        return _gru_cell(msg, states, W_ih, W_hh, b_ih, b_hh)
    x = _layernorm(x + _L0_gnn_ref(x, adj, L0_gnn_W_msg, L0_gnn_b_msg, L0_gnn_W_ih, L0_gnn_W_hh, L0_gnn_b_ih, L0_gnn_b_hh), axis=-1)
    return x

_drawn_inputs = setup_inputs


def setup_inputs(seed=0):
    import zlib

    import numpy as np

    out = dict(_drawn_inputs(seed))
    spreads = {}
    factors = {'L0_gnn_b_msg': 8.0, 'L0_gnn_b_ih': 3.106, 'L0_gnn_b_hh': 4.993}
    for name, (base, spread) in spreads.items():
        noise = np.random.default_rng([zlib.crc32(name.encode()), seed]).standard_normal(out[name].shape)
        drawn = base * np.exp(spread * noise) if base else spread * noise
        out[name] = jnp.asarray(drawn.astype(out[name].dtype))
    for name, factor in factors.items():
        out[name] = (out[name] * factor).astype(out[name].dtype)
    return out
```

```python
import concourse.bass as bass
from concourse import mybir
from contextlib import ExitStack


def gated_graph_layer(nc, x, adj, w_msg, b_msg, w_ih, w_hh, b_ih, b_hh, out):
    fp32 = mybir.dt.float32
    f32r = mybir.dt.float32r
    ALU = mybir.AluOpType
    ACT = mybir.ActivationFunctionType

    LANES = 32
    P = 128
    QUADS = P // LANES
    N, D = x.shape
    SPAN = N // QUADS
    BLOCKS = SPAN // LANES
    PER = 4
    SPLIT = PER - 1
    TILES = BLOCKS // PER
    ROWS = PER * P
    GROUPS = ROWS // LANES
    CHUNKS = 4
    PIECES = BLOCKS // PER
    PIECES_CHUNK = PIECES // CHUNKS
    COLS = PIECES_CHUNK * PER * LANES
    RAW = 2
    RING = 4
    HALVES = 2
    CHUNK_INC = 16 * GROUPS
    EPS = 1e-5
    VE_LOW = (1, 3)

    adj_v = adj.rearrange("(g t b c) (h j) -> g b t h c j", g=QUADS, t=TILES, b=PER, h=QUADS)
    x_v = x.rearrange("(h b c) d -> h c b d", h=QUADS, c=LANES)
    out_v = out.rearrange("(h t b c) d -> b t h c d", h=QUADS, t=TILES, b=PER)

    VE_TILE = len(VE_LOW) * CHUNKS

    def ve_lows(s):
        return s // PIECES_CHUNK * len(VE_LOW) + sum(k < s % PIECES_CHUNK for k in VE_LOW)

    ctx = ExitStack()
    with ctx:
        def sb(name, shape, dt=fp32):
            return ctx.enter_context(nc.sbuf_tensor(name, shape, dt))

        def bank(name):
            return ctx.enter_context(nc.psum_tensor(name, [P, ROWS], fp32))

        def sem(name):
            return ctx.enter_context(nc.semaphore(name))

        raw = sb("raw", [P, RAW, GROUPS, COLS])
        turned = sb("turned", [P, RING, PER, ROWS])
        high = sb("high", [P, HALVES, SPLIT * ROWS], f32r)
        low = sb("low", [P, HALVES, SPLIT * ROWS], f32r)
        x_high = sb("x_high", [P, TILES, SPLIT * D], f32r)
        x_low = sb("x_low", [P, TILES, SPLIT * D], f32r)
        x_whole = sb("x_whole", [P, TILES, D])
        gates = sb("gates", [P, 4, ROWS])
        x_stage = gates[:, :, :]
        sum_a = sb("sum_a", [P, ROWS])
        agg = sb("agg", [P, ROWS])
        msg = sb("msg", [P, ROWS])
        state = sb("state", [P, ROWS])
        x_rows = sb("x_rows", [P, PER, D])
        y = sb("y", [P, PER, D])
        stats = sb("stats", [P, PER, 6])
        moments = sb("moments", [P, PER, 2])
        rstd = sb("rstd", [P, PER])
        var_eps = sb("var_eps", [P, PER])
        eps = sb("eps", [P, PER])
        waited = sb("waited", [P, 1])
        minus_half = sb("minus_half", [P, PER])
        w_rows = sb("w_rows", [P, 7, D])
        w_t = sb("w_t", [P, 7, D])
        ident = sb("ident", [P, P])
        bias_rows = sb("bias_rows", [7, P])
        bias = sb("bias", [P, 7])
        bias_rz = sb("bias_rz", [P, 2])

        ps_a = bank("ps_a")
        ps_b = bank("ps_b")
        ps_m = bank("ps_m")
        ps_h = bank("ps_h")
        ps_r = bank("ps_r")
        ps_z = bank("ps_z")
        ps_in = bank("ps_in")
        ps_hn = bank("ps_hn")

        reset, update, cand, mixed = (gates[:, k, :] for k in range(4))
        W_MSG, W_IR, W_IZ, W_IN, W_HR, W_HZ, W_HN = range(7)

        raw_in = [sem(f"raw_in{k}") for k in range(RAW)]
        x_in = sem("x_in")
        w_in = sem("w_in")
        x_high_done = sem("x_high_done")
        x_low_done = sem("x_low_done")
        piece_turned = sem("piece_turned")
        high_done = sem("high_done")
        low_pool = sem("low_pool")
        low_ve = sem("low_ve")
        high_used = sem("high_used")
        piece_used = sem("piece_used")
        ident_done = sem("ident_done")
        consts_done = sem("consts_done")
        w_turned = sem("w_turned")
        w_done = sem("w_done")
        bias_done = sem("bias_done")
        a_copied = sem("a_copied")
        agg_done = sem("agg_done")
        rows_sum = sem("rows_sum")
        rows_copy = sem("rows_copy")
        state_turned = sem("state_turned")
        state_done = sem("state_done")
        msg_mm = sem("msg_mm")
        msg_done = sem("msg_done")
        r_mm = sem("r_mm")
        z_mm = sem("z_mm")
        n_mm = sem("n_mm")
        r_done = sem("r_done")
        z_done = sem("z_done")
        gated = sem("gated")
        cand_in = sem("cand_in")
        cand_done = sem("cand_done")
        diff_done = sem("diff_done")
        scaled = sem("scaled")
        mixed_done = sem("mixed_done")
        new_turned = sem("new_turned")
        y_done = sem("y_done")
        stats_done = sem("stats_done")
        moments_done = sem("moments_done")
        var_done = sem("var_done")
        rstd_done = sem("rstd_done")
        normed = sem("normed")
        stored = sem("stored")

        block = ctx.enter_context(nc.Block())

        @block.sync
        def _(sp):
            def load_x(q):
                if q:
                    sp.wait_ge(x_high_done, 2 * q)
                    sp.wait_ge(x_low_done, q)
                lo = q * BLOCKS // CHUNKS
                for h in range(QUADS):
                    sp.dma_start(x_stage[LANES * h:LANES * (h + 1), :, :].rearrange("p k (b d) -> p (k b) d", d=D),
                                 x_v[h, :, lo:lo + BLOCKS // CHUNKS, :]).then_inc(x_in, 16)

            def load_chunk(t, q):
                slot = q % RAW
                for g in range(GROUPS):
                    b, quad = g // QUADS, g % QUADS
                    sp.dma_start(raw[:, slot, g, :],
                                 adj_v[quad, b, t, :, :, q * COLS:(q + 1) * COLS]).then_inc(raw_in[slot], 16)

            for q in range(CHUNKS):
                load_x(q)
                if q >= RAW:
                    sp.wait_ge(piece_turned, PIECES_CHUNK * (q - RAW + 1))
                load_chunk(0, q)
            with sp.Fori(1, TILES) as t:
                for q in range(CHUNKS):
                    sp.wait_ge(piece_turned, t * PIECES + PIECES_CHUNK * (q - RAW + 1))
                    load_chunk(t, q)

        @block.vector
        def _(ve):
            def split_x(q):
                ve.wait_ge(x_high_done, 2 * q + 1)
                stage = x_stage.rearrange("p k (b d) -> p k (b d)", d=D)[:, :, 0:SPLIT * D]
                ts = slice(q * TILES // CHUNKS, (q + 1) * TILES // CHUNKS)
                nc.vector.tensor_tensor(x_low[:, ts, :], stage, x_high[:, ts, :].bitcast(fp32),
                                        ALU.subtract).then_inc(x_low_done, 1)

            def turn(t, s, first):
                q, k = divmod(s, PIECES_CHUNK)
                if k == 0:
                    ve.wait_ge(raw_in[q % RAW], CHUNK_INC * (CHUNKS // RAW * t + q // RAW + 1))
                if not first or s >= RING:
                    ve.wait_ge(high_used, PIECES * t + s - RING + 1)
                    ve.wait_ge(low_pool, PIECES * t + s - RING + 1)
                    count = VE_TILE * t + ve_lows(s - RING + 1)
                    if not first or count > 0:
                        ve.wait_ge(low_ve, count)
                src = raw[:, q % RAW, :, k * PER * LANES:(k + 1) * PER * LANES]
                dst = turned[:, s % RING, :, :].rearrange("p b (g c) -> p g b c", c=LANES)
                nc.vector.transpose(dst, src).then_inc(piece_turned, 1)

            def subtract_low(t, s, first):
                if s % PIECES_CHUNK in VE_LOW:
                    ve.wait_ge(high_done, PIECES * t + s + 1)
                    if not first or s >= HALVES:
                        ve.wait_ge(piece_used, PIECES * t + s - HALVES + 1)
                    last = slice((SPLIT - 1) * ROWS, SPLIT * ROWS)
                    nc.vector.tensor_tensor(low[:, s % HALVES, last], turned[:, s % RING, SPLIT - 1, :],
                                            high[:, s % HALVES, last].bitcast(fp32),
                                            ALU.subtract).then_inc(low_ve, 1)

            def gru(u, s):
                if s == 1:
                    ve.wait_ge(piece_used, PIECES * (u + 1))
                    ve.wait_ge(a_copied, u + 1)
                    nc.vector.tensor_tensor(agg[:, :], ps_b[:, :], sum_a[:, :], ALU.add).then_inc(agg_done, 1)
                if s == 6:
                    ve.wait_ge(r_done, u + 1)
                    nc.vector.scalar_tensor_tensor(mixed, ps_hn[:, :], bias[:, W_HN:W_HN + 1], reset,
                                                   ALU.add, ALU.mult).then_inc(gated, 1)
                if s == 7:
                    ve.wait_ge(gated, u + 1)
                    ve.wait_ge(n_mm, u + 1)
                    nc.vector.tensor_tensor(mixed, ps_in[:, :], mixed, ALU.add).then_inc(cand_in, 1)
                if s == 9:
                    ve.wait_ge(cand_done, u + 1)
                    nc.vector.tensor_tensor(mixed, state[:, :], cand, ALU.subtract).then_inc(diff_done, 1)
                if s == 10:
                    ve.wait_ge(diff_done, u + 1)
                    ve.wait_ge(z_done, u + 1)
                    nc.vector.tensor_tensor(mixed, mixed, update, ALU.mult).then_inc(scaled, 1)
                if s == 11:
                    ve.wait_ge(scaled, u + 1)
                    nc.vector.tensor_tensor(mixed, mixed, cand, ALU.add).then_inc(mixed_done, 1)
                if s == 13:
                    ve.wait_ge(new_turned, u + 1)
                    ve.wait_ge(stored, 16 * PER * u)
                    nc.vector.tensor_tensor(y[:, :, :], ps_m[:, :].rearrange("p (b d) -> p b d", d=D),
                                            x_rows[:, :, :], ALU.add).then_inc(y_done, 1)
                    ve.wait_ge(y_done, u + 1)
                    for b in range(PER):
                        nc.vector.bn_stats(stats[:, b, :], y[:, b, :]).then_inc(stats_done, 1)
                    ve.wait_ge(stats_done, PER * (u + 1))
                    nc.vector.tensor_copy(waited[:, :], eps[:, 0:1])
                    for b in range(PER):
                        nc.vector.bn_aggr(moments[:, b, :], stats[:, b, :]).then_inc(moments_done, 1)
                if s == 15:
                    ve.wait_ge(rstd_done, u + 1)
                    for b in range(PER):
                        nc.vector.tensor_scalar(y[:, b, :], y[:, b, :], moments[:, b, 0:1], rstd[:, b:b + 1],
                                                ALU.subtract, ALU.mult).then_inc(normed, 1)

            nc.vector.memset(eps[:, :], EPS).then_inc(consts_done, 1)
            nc.vector.memset(minus_half[:, :], -0.5).then_inc(consts_done, 1)
            split_x(0)
            for s in range(PIECES):
                turn(0, s, True)
                if s:
                    subtract_low(0, s - 1, True)
                if s == 2:
                    ve.wait_ge(w_done, 3)
                    nc.vector.tensor_tensor(bias_rz[:, :], bias[:, W_IR:W_IR + 2], bias[:, W_HR:W_HR + 2],
                                            ALU.add).then_inc(bias_done, 1)
                if s % PIECES_CHUNK == 1 and s // PIECES_CHUNK < CHUNKS - 1:
                    split_x(s // PIECES_CHUNK + 1)
            with ve.Fori(1, TILES) as t:
                for s in range(PIECES):
                    turn(t, s, False)
                    if s:
                        subtract_low(t, s - 1, False)
                    else:
                        subtract_low(t - 1, PIECES - 1, False)
                    gru(t - 1, s)
            subtract_low(TILES - 1, PIECES - 1, False)
            for s in range(PIECES):
                gru(TILES - 1, s)

        @block.scalar
        def _(act):
            act.dma_start(w_rows[:, 0, :], w_msg).then_inc(w_in, 16)
            act.dma_start(w_rows[:, 1:4, :], w_ih.rearrange("(k e) d -> e k d", e=P)).then_inc(w_in, 16)
            act.dma_start(w_rows[:, 4:7, :], w_hh.rearrange("(k e) d -> e k d", e=P)).then_inc(w_in, 16)
            act.dma_start(bias_rows[0:1, :], b_msg.rearrange("(k e) -> k e", k=1)).then_inc(w_in, 16)
            act.dma_start(bias_rows[1:4, :], b_ih.rearrange("(k e) -> k e", e=P)).then_inc(w_in, 16)
            act.dma_start(bias_rows[4:7, :], b_hh.rearrange("(k e) -> k e", e=P)).then_inc(w_in, 16)

            def split_x(q):
                act.wait_ge(x_in, 16 * QUADS * (q + 1))
                stage = x_stage
                ts = slice(q * TILES // CHUNKS, (q + 1) * TILES // CHUNKS)
                nc.scalar.activation(x_high[:, ts, :], stage[:, :, 0:SPLIT * D], ACT.Copy).then_inc(x_high_done, 1)
                nc.scalar.activation(x_whole[:, ts, :], stage[:, :, SPLIT * D:], ACT.Copy).then_inc(x_high_done, 1)

            def round_high(t, s, first):
                act.wait_ge(piece_turned, PIECES * t + s + 1)
                if not first or s >= HALVES:
                    act.wait_ge(high_used, PIECES * t + s - HALVES + 1)
                    act.wait_ge(low_pool, PIECES * t + s - HALVES + 1)
                    count = VE_TILE * t + ve_lows(s - HALVES + 1)
                    if not first or count > 0:
                        act.wait_ge(low_ve, count)
                nc.scalar.activation(high[:, s % HALVES, :],
                                     turned[:, s % RING, 0:SPLIT, :].rearrange("p b r -> p (b r)"),
                                     ACT.Copy).then_inc(high_done, 1)

            def gru(u, s):
                if s == 0:
                    if not isinstance(u, int) or u:
                        act.wait_ge(y_done, u)
                        act.wait_ge(state_turned, u)
                    nc.scalar.activation(x_rows[:, SPLIT:PER, :], x_whole[:, bass.ds(u, 1), :],
                                         ACT.Copy).then_inc(rows_copy, 1)
                if s == 2:
                    act.wait_ge(state_turned, u + 1)
                    if not isinstance(u, int) or u:
                        act.wait_ge(diff_done, u)
                    nc.scalar.activation(state[:, :], ps_h[:, :], ACT.Copy).then_inc(state_done, 1)
                if s == 3:
                    act.wait_ge(msg_mm, u + 1)
                    if not isinstance(u, int) or u:
                        act.wait_ge(n_mm, u)
                    nc.scalar.activation(msg[:, :], ps_m[:, :], ACT.Relu, bias=bias[:, 0:1]).then_inc(msg_done, 1)
                if s == 5:
                    act.wait_ge(r_mm, u + 1)
                    if not isinstance(u, int) or u:
                        act.wait_ge(gated, u)
                    nc.scalar.activation(reset, ps_r[:, :], ACT.Sigmoid, bias=bias_rz[:, 0:1]).then_inc(r_done, 1)
                if s == 6:
                    act.wait_ge(z_mm, u + 1)
                    if not isinstance(u, int) or u:
                        act.wait_ge(scaled, u)
                    nc.scalar.activation(update, ps_z[:, :], ACT.Sigmoid, bias=bias_rz[:, 1:2]).then_inc(z_done, 1)
                if s == 8:
                    act.wait_ge(cand_in, u + 1)
                    if not isinstance(u, int) or u:
                        act.wait_ge(mixed_done, u)
                    nc.scalar.activation(cand, mixed, ACT.Tanh, bias=bias[:, W_IN:W_IN + 1]).then_inc(cand_done, 1)
                if s == PIECES:
                    act.wait_ge(normed, PER * (u + 1))
                    for b in range(PER):
                        act.dma_start(out_v[b, u], y[:, b, :]).then_inc(stored, 16)

            def copy_a(t, s):
                if s == PIECES // 2 + 2:
                    act.wait_ge(piece_used, PIECES * t + PIECES // 2)
                    if not isinstance(t, int) or t:
                        act.wait_ge(agg_done, t)
                    nc.scalar.activation(sum_a[:, :], ps_a[:, :], ACT.Copy).then_inc(a_copied, 1)

            split_x(0)
            for s in range(PIECES):
                round_high(0, s, True)
                copy_a(0, s)
                if s == 2:
                    act.wait_ge(w_turned, 1)
                    nc.scalar.activation(w_t[:, 0:4, :].rearrange("p k d -> p (k d)"), ps_h[:, :],
                                         ACT.Copy).then_inc(w_done, 1)
                    nc.scalar.activation(w_t[:, 4:7, :].rearrange("p k d -> p (k d)"), ps_m[:, 0:3 * D],
                                         ACT.Copy).then_inc(w_done, 1)
                    nc.scalar.activation(bias[:, :], ps_m[:, 3 * D:3 * D + 7], ACT.Copy).then_inc(w_done, 1)
                if s % PIECES_CHUNK == 1 and s // PIECES_CHUNK < CHUNKS - 1:
                    split_x(s // PIECES_CHUNK + 1)
            with act.Fori(1, TILES) as t:
                for s in range(PIECES):
                    round_high(t, s, False)
                    copy_a(t, s)
                    gru(t - 1, s)
                gru(t - 1, PIECES)
            for s in range(PIECES + 1):
                gru(TILES - 1, s)
            act.wait_ge(stored, 16 * PER * TILES)

        @block.gpsimd
        def _(pool):
            nc.gpsimd.memset(ident[:, :], 0.0).then_inc(ident_done, 1)
            pool.wait_ge(ident_done, 1)
            nc.gpsimd.affine_select(out=ident[:, :], in_=ident[:, :], compare_op=ALU.not_equal, fill=1.0, base=0,
                                    pattern=[[-1, P]], channel_multiplier=1).then_inc(ident_done, 1)

            def subtract_low(t, s, first):
                pool.wait_ge(high_done, PIECES * t + s + 1)
                if not first or s >= HALVES:
                    pool.wait_ge(piece_used, PIECES * t + s - HALVES + 1)
                n = (SPLIT - (s % PIECES_CHUNK in VE_LOW)) * ROWS
                nc.gpsimd.tensor_tensor(low[:, s % HALVES, 0:n],
                                        turned[:, s % RING, :, :].rearrange("p b r -> p (b r)")[:, 0:n],
                                        high[:, s % HALVES, 0:n].bitcast(fp32),
                                        ALU.subtract).then_inc(low_pool, 1)

            def gru(u, s):
                if s == 0:
                    if not isinstance(u, int) or u:
                        pool.wait_ge(y_done, u)
                        pool.wait_ge(state_turned, u)
                    t1 = bass.ds(u, 1)
                    nc.gpsimd.tensor_tensor(x_rows[:, 0:SPLIT, :].rearrange("p b d -> p (b d)").rearrange("p (o n) -> p o n", o=1),
                                            x_high[:, t1, :].bitcast(fp32), x_low[:, t1, :].bitcast(fp32),
                                            ALU.add).then_inc(rows_sum, 1)
                if s == 14:
                    pool.wait_ge(moments_done, PER * (u + 1))
                    if not isinstance(u, int) or u:
                        pool.wait_ge(normed, PER * u)
                    nc.gpsimd.tensor_tensor(var_eps[:, :], moments[:, :, 1], eps[:, :], ALU.add).then_inc(var_done, 1)
                    pool.wait_ge(var_done, u + 1)
                    nc.gpsimd.tensor_tensor(rstd[:, :], var_eps[:, :], minus_half[:, :], ALU.pow).then_inc(rstd_done, 1)

            pool.wait_ge(consts_done, 2)
            for s in range(PIECES):
                subtract_low(0, s, True)
            with pool.Fori(1, TILES) as t:
                for s in range(PIECES):
                    subtract_low(t, s, False)
                    gru(t - 1, s)
            for s in range(PIECES):
                gru(TILES - 1, s)

        @block.tensor
        def _(pe):
            def products(t, s, first):
                ps = ps_a if s < PIECES // 2 else ps_b
                if s % (PIECES // 2) == 0 and not first:
                    if s == 0:
                        pe.wait_ge(a_copied, t)
                    else:
                        pe.wait_ge(agg_done, t)
                if first and s % PIECES_CHUNK == 0:
                    pe.wait_ge(x_high_done, 2 * (s // PIECES_CHUNK + 1))
                    pe.wait_ge(x_low_done, s // PIECES_CHUNK + 1)
                pe.wait_ge(piece_turned, PIECES * t + s + 1)
                nc.tensor.matmul(ps[:, :], x_whole[:, s, :], turned[:, s % RING, SPLIT, :],
                                 start=(s % (PIECES // 2) == 0), stop=False)
                pe.wait_ge(high_done, PIECES * t + s + 1)
                for b in range(SPLIT):
                    rhs = high[:, s % HALVES, b * ROWS:(b + 1) * ROWS]
                    nc.tensor.matmul(ps[:, :], x_low[:, s, b * D:(b + 1) * D], rhs, start=False, stop=False)
                    last = nc.tensor.matmul(ps[:, :], x_high[:, s, b * D:(b + 1) * D], rhs, start=False, stop=False)
                last.then_inc(high_used, 1)

            def low_products(t, s):
                ps = ps_a if s < PIECES // 2 else ps_b
                stop = s % (PIECES // 2) == PIECES // 2 - 1
                pe.wait_ge(low_pool, PIECES * t + s + 1)
                for b in range(SPLIT):
                    if b == SPLIT - 1 and s % PIECES_CHUNK in VE_LOW:
                        pe.wait_ge(low_ve, VE_TILE * t + ve_lows(s + 1))
                    last = nc.tensor.matmul(ps[:, :], x_high[:, s, b * D:(b + 1) * D], low[:, s % HALVES, b * ROWS:(b + 1) * ROWS],
                                            start=False, stop=stop and b == SPLIT - 1)
                last.then_inc(piece_used, 1)

            def gru(u, s):
                if s == 1:
                    pe.wait_ge(rows_sum, u + 1)
                    pe.wait_ge(rows_copy, u + 1)
                    for b in range(PER):
                        last = nc.tensor.transpose(ps_h[:, b * P:(b + 1) * P], x_rows[:, b, :], ident[:, :])
                    last.then_inc(state_turned, 1)
                if s == 2:
                    pe.wait_ge(agg_done, u + 1)
                    nc.tensor.matmul(ps_m[:, :], w_t[:, W_MSG, :], agg[:, :], start=True, stop=True).then_inc(msg_mm, 1)
                if s == 3:
                    pe.wait_ge(state_done, u + 1)
                    nc.tensor.matmul(ps_hn[:, :], w_t[:, W_HN, :], state[:, :], start=True, stop=True)
                if s == 4:
                    pe.wait_ge(msg_done, u + 1)
                    nc.tensor.matmul(ps_r[:, :], w_t[:, W_HR, :], state[:, :], start=True, stop=False)
                    nc.tensor.matmul(ps_r[:, :], w_t[:, W_IR, :], msg[:, :], start=False, stop=True).then_inc(r_mm, 1)
                if s == 5:
                    nc.tensor.matmul(ps_z[:, :], w_t[:, W_HZ, :], state[:, :], start=True, stop=False)
                    nc.tensor.matmul(ps_z[:, :], w_t[:, W_IZ, :], msg[:, :], start=False, stop=True).then_inc(z_mm, 1)
                if s == 6:
                    nc.tensor.matmul(ps_in[:, :], w_t[:, W_IN, :], msg[:, :], start=True, stop=True).then_inc(n_mm, 1)
                if s == 12:
                    pe.wait_ge(mixed_done, u + 1)
                    for b in range(PER):
                        last = nc.tensor.transpose(ps_m[:, b * P:(b + 1) * P], mixed[:, b * P:(b + 1) * P], ident[:, :])
                    last.then_inc(new_turned, 1)

            pe.wait_ge(ident_done, 2)
            pe.wait_ge(w_in, 16 * 6)
            for k in range(7):
                dst = ps_h[:, k * D:(k + 1) * D] if k < 4 else ps_m[:, (k - 4) * D:(k - 3) * D]
                last = nc.tensor.transpose(dst, w_rows[:, k, :], ident[:, :])
            nc.tensor.transpose(ps_m[:, 3 * D:3 * D + 7], bias_rows[:, :], ident[0:7, 0:7]).then_inc(w_turned, 1)
            for s in range(PIECES):
                products(0, s, True)
                if s:
                    low_products(0, s - 1)
            pe.wait_ge(w_done, 3)
            with pe.Fori(1, TILES) as t:
                for s in range(PIECES):
                    products(t, s, False)
                    low_products(t - 1, PIECES - 1) if s == 0 else low_products(t, s - 1)
                    gru(t - 1, s)
            low_products(TILES - 1, PIECES - 1)
            for s in range(PIECES):
                gru(TILES - 1, s)


_INS = ["x", "adj", "L0_gnn_W_msg", "L0_gnn_b_msg", "L0_gnn_W_ih", "L0_gnn_W_hh", "L0_gnn_b_ih", "L0_gnn_b_hh"]


def kernel(**inputs):
    import numpy as _np
    import concourse.bacc as _bacc
    from concourse import mybir as _mybir
    from concourse.bass_utils import run_bass_kernel_spmd as _run

    nc = _bacc.Bacc("TRN2", target_bir_lowering=False, num_devices=1)
    arrays, args = {}, []
    for name in _INS:
        a = _np.ascontiguousarray(inputs[name])
        arrays[f"in_{name}"] = a
        args.append(nc.dram_tensor(f"in_{name}", a.shape, _mybir.dt.from_np(a.dtype), kind="ExternalInput").ap())
    out = nc.dram_tensor("out", inputs["x"].shape, _mybir.dt.float32, kind="ExternalOutput").ap()
    gated_graph_layer(nc, *args, out)
    r = _run(nc, [arrays], core_ids=[0])
    return r.results[0]["out"]
```

```python
import concourse.bass as bass
from concourse import mybir
from contextlib import ExitStack


def gated_graph_layer(nc, x, adj, w_msg, b_msg, w_ih, w_hh, b_ih, b_hh, out):
    fp32 = mybir.dt.float32
    f32r = mybir.dt.float32r
    ALU = mybir.AluOpType
    ACT = mybir.ActivationFunctionType

    LANES = 32
    P = 128
    QUADS = P // LANES
    N, D = x.shape
    SPAN = N // QUADS
    BLOCKS = SPAN // LANES
    PER = 4
    SPLIT = PER - 1
    TILES = BLOCKS // PER
    ROWS = PER * P
    GROUPS = ROWS // LANES
    CHUNKS = 4
    PIECES = BLOCKS // PER
    PIECES_CHUNK = PIECES // CHUNKS
    COLS = PIECES_CHUNK * PER * LANES
    RAW = 2
    RING = 4
    HALVES = 2
    CHUNK_INC = 16 * GROUPS
    EPS = 1e-5
    VE_LAG = 3
    VE_LOW = (1, 3)

    adj_v = adj.rearrange("(g t b c) (h j) -> g b t h c j", g=QUADS, t=TILES, b=PER, h=QUADS)
    x_v = x.rearrange("(h b c) d -> h c b d", h=QUADS, c=LANES)
    out_v = out.rearrange("(h t b c) d -> b t h c d", h=QUADS, t=TILES, b=PER)

    VE_TILE = len(VE_LOW) * CHUNKS

    def ve_lows(s):
        return s // PIECES_CHUNK * len(VE_LOW) + sum(k < s % PIECES_CHUNK for k in VE_LOW)

    ctx = ExitStack()
    with ctx:
        def sb(name, shape, dt=fp32):
            return ctx.enter_context(nc.sbuf_tensor(name, shape, dt))

        def bank(name):
            return ctx.enter_context(nc.psum_tensor(name, [P, ROWS], fp32))

        def sem(name):
            return ctx.enter_context(nc.semaphore(name))

        raw = sb("raw", [P, RAW, GROUPS, COLS])
        turned = sb("turned", [P, RING, PER, ROWS])
        high = sb("high", [P, HALVES, SPLIT * ROWS], f32r)
        low = sb("low", [P, HALVES, SPLIT * ROWS], f32r)
        x_high = sb("x_high", [P, TILES, SPLIT * D], f32r)
        x_low = sb("x_low", [P, TILES, SPLIT * D], f32r)
        x_whole = sb("x_whole", [P, TILES, D])
        gates = sb("gates", [P, 4, ROWS])
        x_stage = gates[:, :, :]
        sum_a = sb("sum_a", [P, ROWS])
        half_hn = sb("half_hn", [P, ROWS])
        agg = sb("agg", [P, ROWS])
        msg = sb("msg", [P, ROWS])
        state = sb("state", [P, ROWS])
        x_rows = sb("x_rows", [P, PER, D])
        y = sb("y", [P, PER, D])
        stats = sb("stats", [P, PER, 6])
        moments = sb("moments", [P, PER, 2])
        rstd = sb("rstd", [P, PER])
        var_eps = sb("var_eps", [P, PER])
        eps = sb("eps", [P, PER])
        waited = sb("waited", [P, 1])
        zero = sb("zero", [P, PER])
        minus_mean = sb("minus_mean", [P, PER])
        shift = sb("shift", [P, PER])
        minus_half = sb("minus_half", [P, PER])
        w_rows = sb("w_rows", [P, 7, D])
        w_t = sb("w_t", [P, 7, D])
        ident = sb("ident", [P, P])
        bias_rows = sb("bias_rows", [7, P])
        bias = sb("bias", [P, 7])
        half_bias = sb("half_bias", [P, 3])

        ps_a = bank("ps_a")
        ps_b = bank("ps_b")
        ps_m = bank("ps_m")
        ps_h = bank("ps_h")
        ps_r = bank("ps_r")
        ps_z = bank("ps_z")
        ps_in = bank("ps_in")
        ps_hn = bank("ps_hn")

        reset, update, cand, mixed = (gates[:, k, :] for k in range(4))
        W_MSG, W_IR, W_IZ, W_IN, W_HR, W_HZ, W_HN = range(7)

        raw_in = [sem(f"raw_in{k}") for k in range(RAW)]
        x_in = sem("x_in")
        w_in = sem("w_in")
        x_high_done = sem("x_high_done")
        x_low_done = sem("x_low_done")
        piece_turned = sem("piece_turned")
        high_done = sem("high_done")
        low_pool = sem("low_pool")
        low_ve = sem("low_ve")
        high_used = sem("high_used")
        piece_used = sem("piece_used")
        ident_done = sem("ident_done")
        consts_done = sem("consts_done")
        w_turned = sem("w_turned")
        w_done = sem("w_done")
        bias_done = sem("bias_done")
        a_copied = sem("a_copied")
        agg_done = sem("agg_done")
        rows_sum = sem("rows_sum")
        rows_copy = sem("rows_copy")
        state_turned = sem("state_turned")
        state_done = sem("state_done")
        msg_mm = sem("msg_mm")
        msg_done = sem("msg_done")
        r_mm = sem("r_mm")
        z_mm = sem("z_mm")
        n_mm = sem("n_mm")
        hn_done = sem("hn_done")
        r_done = sem("r_done")
        z_done = sem("z_done")
        gated = sem("gated")
        cand_in = sem("cand_in")
        cand_done = sem("cand_done")
        diff_done = sem("diff_done")
        scaled = sem("scaled")
        mixed_done = sem("mixed_done")
        hn_mm = sem("hn_mm")
        total_done = sem("total_done")
        sum_turned = sem("sum_turned")
        stats_done = sem("stats_done")
        moments_done = sem("moments_done")
        var_done = sem("var_done")
        rstd_done = sem("rstd_done")
        mean_done = sem("mean_done")
        shift_done = sem("shift_done")
        normed = sem("normed")
        stored = sem("stored")

        block = ctx.enter_context(nc.Block())

        @block.sync
        def _(sp):
            def load_x(q):
                if q:
                    sp.wait_ge(x_high_done, 2 * q)
                    sp.wait_ge(x_low_done, q)
                lo = q * BLOCKS // CHUNKS
                for h in range(QUADS):
                    sp.dma_start(x_stage[LANES * h:LANES * (h + 1), :, :].rearrange("p k (b d) -> p (k b) d", d=D),
                                 x_v[h, :, lo:lo + BLOCKS // CHUNKS, :]).then_inc(x_in, 16)

            def load_chunk(t, q):
                slot = q % RAW
                for g in range(GROUPS):
                    b, quad = g // QUADS, g % QUADS
                    sp.dma_start(raw[:, slot, g, :],
                                 adj_v[quad, b, t, :, :, q * COLS:(q + 1) * COLS]).then_inc(raw_in[slot], 16)

            def next_chunk(t, q):
                sp.wait_ge(piece_turned, PIECES * t + PIECES_CHUNK * (q - RAW + 1))
                load_chunk(t, q)

            def store(u):
                sp.wait_ge(normed, PER * (u + 1))
                for b in range(PER):
                    sp.dma_start(out_v[b, u], y[:, b, :]).then_inc(stored, 16)

            for q in range(CHUNKS):
                load_x(q)
                if q >= RAW:
                    sp.wait_ge(piece_turned, PIECES_CHUNK * (q - RAW + 1))
                load_chunk(0, q)
            for q in range(CHUNKS):
                next_chunk(1, q)
            with sp.Fori(2, TILES) as t:
                for q in range(CHUNKS):
                    if q == 2:
                        store(t - 2)
                    next_chunk(t, q)
            store(TILES - 2)
            store(TILES - 1)
            sp.wait_ge(stored, 16 * PER * TILES)

        @block.vector
        def _(ve):
            def split_x(q):
                ve.wait_ge(x_high_done, 2 * q + 1)
                stage = x_stage.rearrange("p k (b d) -> p k (b d)", d=D)[:, :, 0:SPLIT * D]
                ts = slice(q * TILES // CHUNKS, (q + 1) * TILES // CHUNKS)
                nc.vector.tensor_tensor(x_low[:, ts, :], stage, x_high[:, ts, :].bitcast(fp32),
                                        ALU.subtract).then_inc(x_low_done, 1)

            def turn(t, s, first):
                q, k = divmod(s, PIECES_CHUNK)
                if k == 0:
                    ve.wait_ge(raw_in[q % RAW], CHUNK_INC * (CHUNKS // RAW * t + q // RAW + 1))
                if not first or s >= RING:
                    ve.wait_ge(high_used, PIECES * t + s - RING + 1)
                    ve.wait_ge(low_pool, PIECES * t + s - RING + 1)
                    count = VE_TILE * t + ve_lows(s - RING + 1)
                    if not first or count > 0:
                        ve.wait_ge(low_ve, count)
                src = raw[:, q % RAW, :, k * PER * LANES:(k + 1) * PER * LANES]
                dst = turned[:, s % RING, :, :].rearrange("p b (g c) -> p g b c", c=LANES)
                nc.vector.transpose(dst, src).then_inc(piece_turned, 1)

            def subtract_low(t, s, first):
                if s % PIECES_CHUNK in VE_LOW:
                    ve.wait_ge(high_done, PIECES * t + s + 1)
                    if not first or s >= HALVES:
                        ve.wait_ge(piece_used, PIECES * t + s - HALVES + 1)
                    last = slice((SPLIT - 1) * ROWS, SPLIT * ROWS)
                    nc.vector.tensor_tensor(low[:, s % HALVES, last], turned[:, s % RING, SPLIT - 1, :],
                                            high[:, s % HALVES, last].bitcast(fp32),
                                            ALU.subtract).then_inc(low_ve, 1)

            def gru(u, s):
                if s == 4:
                    ve.wait_ge(piece_used, PIECES * (u + 1))
                    ve.wait_ge(a_copied, u + 1)
                    nc.vector.tensor_tensor(agg[:, :], ps_b[:, :], sum_a[:, :], ALU.add).then_inc(agg_done, 1)
                if s == 9:
                    ve.wait_ge(r_done, u + 1)
                    nc.vector.scalar_tensor_tensor(mixed, reset, 1.0, half_hn[:, :],
                                                   ALU.add, ALU.mult).then_inc(gated, 1)
                if s == 10:
                    ve.wait_ge(gated, u + 1)
                    ve.wait_ge(n_mm, u + 1)
                    nc.vector.tensor_tensor(mixed, ps_in[:, :], mixed, ALU.add).then_inc(cand_in, 1)
                if s == 12:
                    ve.wait_ge(cand_done, u + 1)
                    nc.vector.tensor_tensor(mixed, state[:, :], cand, ALU.subtract).then_inc(diff_done, 1)
                    ve.wait_ge(diff_done, u + 1)
                    ve.wait_ge(z_done, u + 1)
                    nc.vector.scalar_tensor_tensor(mixed, update, 1.0, mixed, ALU.add, ALU.mult).then_inc(scaled, 1)
                    ve.wait_ge(scaled, u + 1)
                    nc.vector.scalar_tensor_tensor(mixed, mixed, 0.5, cand, ALU.mult, ALU.add).then_inc(mixed_done, 1)
                    ve.wait_ge(mixed_done, u + 1)
                    nc.vector.tensor_tensor(mixed, mixed, state[:, :], ALU.add).then_inc(total_done, 1)
                if s == 15:
                    ve.wait_ge(sum_turned, u + 1)
                    for b in range(PER):
                        nc.vector.bn_stats(stats[:, b, :], ps_m[:, b * D:(b + 1) * D]).then_inc(stats_done, 1)
                    ve.wait_ge(stats_done, PER * (u + 1))
                    nc.vector.tensor_copy(waited[:, :], eps[:, 0:1])
                    for b in range(PER):
                        nc.vector.bn_aggr(moments[:, b, :], stats[:, b, :]).then_inc(moments_done, 1)

            nc.vector.memset(zero[:, :], 0.0).then_inc(consts_done, 1)
            nc.vector.memset(eps[:, :], EPS).then_inc(consts_done, 1)
            nc.vector.memset(minus_half[:, :], -0.5).then_inc(consts_done, 1)
            split_x(0)
            for s in range(PIECES):
                turn(0, s, True)
                if s >= VE_LAG:
                    subtract_low(0, s - VE_LAG, True)
                if s == 2:
                    ve.wait_ge(w_done, 3)
                    nc.vector.tensor_tensor(half_bias[:, 0:2], bias[:, W_IR:W_IR + 2], bias[:, W_HR:W_HR + 2],
                                            ALU.add).then_inc(bias_done, 1)
                    nc.vector.tensor_copy(half_bias[:, 2:3], bias[:, W_HN:W_HN + 1]).then_inc(bias_done, 1)
                    ve.wait_ge(bias_done, 2)
                    nc.vector.tensor_scalar(half_bias[:, :], half_bias[:, :], 0.5, None,
                                            ALU.mult).then_inc(bias_done, 1)
                if s % PIECES_CHUNK == PIECES_CHUNK - 1 and s // PIECES_CHUNK < CHUNKS - 1:
                    split_x(s // PIECES_CHUNK + 1)
            with ve.Fori(1, TILES) as t:
                for s in range(PIECES):
                    turn(t, s, False)
                    if s >= VE_LAG:
                        subtract_low(t, s - VE_LAG, False)
                    else:
                        subtract_low(t - 1, PIECES + s - VE_LAG, False)
                    gru(t - 1, s)
            for s in range(PIECES - VE_LAG, PIECES):
                subtract_low(TILES - 1, s, False)
            for s in range(PIECES):
                gru(TILES - 1, s)

        @block.scalar
        def _(act):
            act.dma_start(w_rows[:, 0, :], w_msg).then_inc(w_in, 16)
            act.dma_start(w_rows[:, 1:4, :], w_ih.rearrange("(k e) d -> e k d", e=P)).then_inc(w_in, 16)
            act.dma_start(w_rows[:, 4:7, :], w_hh.rearrange("(k e) d -> e k d", e=P)).then_inc(w_in, 16)
            act.dma_start(bias_rows[0:1, :], b_msg.rearrange("(k e) -> k e", k=1)).then_inc(w_in, 16)
            act.dma_start(bias_rows[1:4, :], b_ih.rearrange("(k e) -> k e", e=P)).then_inc(w_in, 16)
            act.dma_start(bias_rows[4:7, :], b_hh.rearrange("(k e) -> k e", e=P)).then_inc(w_in, 16)

            def split_x(q):
                act.wait_ge(x_in, 16 * QUADS * (q + 1))
                stage = x_stage
                ts = slice(q * TILES // CHUNKS, (q + 1) * TILES // CHUNKS)
                nc.scalar.activation(x_high[:, ts, :], stage[:, :, 0:SPLIT * D], ACT.Copy).then_inc(x_high_done, 1)
                nc.scalar.activation(x_whole[:, ts, :], stage[:, :, SPLIT * D:], ACT.Copy).then_inc(x_high_done, 1)

            def round_high(t, s, first):
                act.wait_ge(piece_turned, PIECES * t + s + 1)
                if not first or s >= HALVES:
                    act.wait_ge(high_used, PIECES * t + s - HALVES + 1)
                    act.wait_ge(low_pool, PIECES * t + s - HALVES + 1)
                    count = VE_TILE * t + ve_lows(s - HALVES + 1)
                    if not first or count > 0:
                        act.wait_ge(low_ve, count)
                nc.scalar.activation(high[:, s % HALVES, :],
                                     turned[:, s % RING, 0:SPLIT, :].rearrange("p b r -> p (b r)"),
                                     ACT.Copy).then_inc(high_done, 1)

            def early(t, s):
                if s == 8:
                    if not isinstance(t, int) or t:
                        act.wait_ge(state_turned, t)
                    nc.scalar.activation(x_rows[:, SPLIT:PER, :], x_whole[:, bass.ds(t, 1), :],
                                         ACT.Copy).then_inc(rows_copy, 1)
                if s == 12:
                    act.wait_ge(state_turned, t + 1)
                    if not isinstance(t, int) or t:
                        act.wait_ge(total_done, t)
                    nc.scalar.activation(state[:, :], ps_h[:, :], ACT.Copy).then_inc(state_done, 1)
                if s == 15:
                    act.wait_ge(hn_mm, t + 1)
                    if not isinstance(t, int) or t:
                        act.wait_ge(gated, t)
                    nc.scalar.activation(half_hn[:, :], ps_hn[:, :], ACT.Identity, bias=half_bias[:, 2:3],
                                         scale=0.5).then_inc(hn_done, 1)

            def gru(u, s):
                if s == 4:
                    act.wait_ge(msg_mm, u + 1)
                    if not isinstance(u, int) or u:
                        act.wait_ge(n_mm, u)
                    nc.scalar.activation(msg[:, :], ps_m[:, :], ACT.Relu, bias=bias[:, 0:1]).then_inc(msg_done, 1)
                if s == 6:
                    act.wait_ge(r_mm, u + 1)
                    nc.scalar.activation(reset, ps_r[:, :], ACT.Tanh, bias=half_bias[:, 0:1],
                                         scale=0.5).then_inc(r_done, 1)
                if s == 7:
                    act.wait_ge(z_mm, u + 1)
                    if not isinstance(u, int) or u:
                        act.wait_ge(scaled, u)
                    nc.scalar.activation(update, ps_z[:, :], ACT.Tanh, bias=half_bias[:, 1:2],
                                         scale=0.5).then_inc(z_done, 1)
                if s == 9:
                    act.wait_ge(cand_in, u + 1)
                    nc.scalar.activation(cand, mixed, ACT.Tanh, bias=bias[:, W_IN:W_IN + 1]).then_inc(cand_done, 1)
                if s == 15:
                    act.wait_ge(shift_done, u + 1)
                    if not isinstance(u, int) or u:
                        act.wait_ge(stored, 16 * PER * u)
                    for b in range(PER):
                        nc.scalar.activation(y[:, b, :], ps_m[:, b * D:(b + 1) * D], ACT.Identity,
                                             bias=shift[:, b:b + 1], scale=rstd[:, b:b + 1]).then_inc(normed, 1)

            def copy_a(t, s):
                if s == PIECES // 2 + 2:
                    act.wait_ge(piece_used, PIECES * t + PIECES // 2)
                    if not isinstance(t, int) or t:
                        act.wait_ge(agg_done, t)
                    nc.scalar.activation(sum_a[:, :], ps_a[:, :], ACT.Copy).then_inc(a_copied, 1)

            split_x(0)
            for s in range(PIECES):
                round_high(0, s, True)
                copy_a(0, s)
                early(0, s)
                if s == 6:
                    act.wait_ge(bias_done, 3)
                if s == 2:
                    act.wait_ge(w_turned, 1)
                    nc.scalar.activation(w_t[:, 0:4, :].rearrange("p k d -> p (k d)"), ps_h[:, :],
                                         ACT.Copy).then_inc(w_done, 1)
                    nc.scalar.activation(w_t[:, 4:7, :].rearrange("p k d -> p (k d)"), ps_m[:, 0:3 * D],
                                         ACT.Copy).then_inc(w_done, 1)
                    nc.scalar.activation(bias[:, :], ps_m[:, 3 * D:3 * D + 7], ACT.Copy).then_inc(w_done, 1)
                if s % PIECES_CHUNK == 1 and s // PIECES_CHUNK < CHUNKS - 1:
                    split_x(s // PIECES_CHUNK + 1)
            with act.Fori(1, TILES) as t:
                for s in range(PIECES):
                    round_high(t, s, False)
                    copy_a(t, s)
                    gru(t - 1, s)
                    early(t, s)
            for s in range(PIECES):
                gru(TILES - 1, s)

        @block.gpsimd
        def _(pool):
            nc.gpsimd.memset(ident[:, :], 0.0).then_inc(ident_done, 1)
            pool.wait_ge(ident_done, 1)
            nc.gpsimd.affine_select(out=ident[:, :], in_=ident[:, :], compare_op=ALU.not_equal, fill=1.0, base=0,
                                    pattern=[[-1, P]], channel_multiplier=1).then_inc(ident_done, 1)

            def subtract_low(t, s, first):
                pool.wait_ge(high_done, PIECES * t + s + 1)
                if not first or s >= HALVES:
                    pool.wait_ge(piece_used, PIECES * t + s - HALVES + 1)
                n = (SPLIT - (s % PIECES_CHUNK in VE_LOW)) * ROWS
                nc.gpsimd.tensor_tensor(low[:, s % HALVES, 0:n],
                                        turned[:, s % RING, :, :].rearrange("p b r -> p (b r)")[:, 0:n],
                                        high[:, s % HALVES, 0:n].bitcast(fp32),
                                        ALU.subtract).then_inc(low_pool, 1)

            def early(t, s):
                if s == 8:
                    if not isinstance(t, int) or t:
                        pool.wait_ge(state_turned, t)
                    t1 = bass.ds(t, 1)
                    rows = x_rows[:, 0:SPLIT, :].rearrange("p b d -> p (b d)").rearrange("p (o n) -> p o n", o=1)
                    nc.gpsimd.tensor_tensor(rows, x_high[:, t1, :].bitcast(fp32), x_low[:, t1, :].bitcast(fp32),
                                            ALU.add).then_inc(rows_sum, 1)

            def gru(u, s):
                if s == 13:
                    pool.wait_ge(moments_done, PER * (u + 1))
                    if not isinstance(u, int) or u:
                        pool.wait_ge(normed, PER * u)
                    nc.gpsimd.tensor_tensor(var_eps[:, :], moments[:, :, 1], eps[:, :], ALU.add).then_inc(var_done, 1)
                    pool.wait_ge(var_done, u + 1)
                    nc.gpsimd.tensor_tensor(rstd[:, :], var_eps[:, :], minus_half[:, :], ALU.pow).then_inc(rstd_done, 1)
                    pool.wait_ge(rstd_done, u + 1)
                    nc.gpsimd.tensor_tensor(minus_mean[:, :], zero[:, :], moments[:, :, 0], ALU.subtract).then_inc(mean_done, 1)
                    pool.wait_ge(mean_done, u + 1)
                    nc.gpsimd.tensor_tensor(shift[:, :], minus_mean[:, :], rstd[:, :], ALU.mult).then_inc(shift_done, 1)

            pool.wait_ge(consts_done, 3)
            for s in range(PIECES):
                subtract_low(0, s, True)
                early(0, s)
            with pool.Fori(1, TILES) as t:
                for s in range(PIECES):
                    subtract_low(t, s, False)
                    gru(t - 1, s)
                    early(t, s)
            for s in range(PIECES):
                gru(TILES - 1, s)

        @block.tensor
        def _(pe):
            def products(t, s, first):
                ps = ps_a if s < PIECES // 2 else ps_b
                if s % (PIECES // 2) == 0 and not first:
                    if s == 0:
                        pe.wait_ge(a_copied, t)
                    else:
                        pe.wait_ge(agg_done, t)
                if first and s % PIECES_CHUNK == 0:
                    pe.wait_ge(x_high_done, 2 * (s // PIECES_CHUNK + 1))
                    pe.wait_ge(x_low_done, s // PIECES_CHUNK + 1)
                pe.wait_ge(piece_turned, PIECES * t + s + 1)
                nc.tensor.matmul(ps[:, :], x_whole[:, s, :], turned[:, s % RING, SPLIT, :],
                                 start=(s % (PIECES // 2) == 0), stop=False)
                pe.wait_ge(high_done, PIECES * t + s + 1)
                for b in range(SPLIT):
                    rhs = high[:, s % HALVES, b * ROWS:(b + 1) * ROWS]
                    nc.tensor.matmul(ps[:, :], x_low[:, s, b * D:(b + 1) * D], rhs, start=False, stop=False)
                    last = nc.tensor.matmul(ps[:, :], x_high[:, s, b * D:(b + 1) * D], rhs, start=False, stop=False)
                last.then_inc(high_used, 1)

            def low_products(t, s):
                ps = ps_a if s < PIECES // 2 else ps_b
                stop = s % (PIECES // 2) == PIECES // 2 - 1
                pe.wait_ge(low_pool, PIECES * t + s + 1)
                for b in range(SPLIT):
                    if b == SPLIT - 1 and s % PIECES_CHUNK in VE_LOW:
                        pe.wait_ge(low_ve, VE_TILE * t + ve_lows(s + 1))
                    last = nc.tensor.matmul(ps[:, :], x_high[:, s, b * D:(b + 1) * D], low[:, s % HALVES, b * ROWS:(b + 1) * ROWS],
                                            start=False, stop=stop and b == SPLIT - 1)
                last.then_inc(piece_used, 1)

            def early(t, s):
                if s == 9:
                    pe.wait_ge(rows_sum, t + 1)
                    pe.wait_ge(rows_copy, t + 1)
                    if not isinstance(t, int) or t:
                        pe.wait_ge(state_done, t)
                    for b in range(PER):
                        last = nc.tensor.transpose(ps_h[:, b * P:(b + 1) * P], x_rows[:, b, :], ident[:, :])
                    last.then_inc(state_turned, 1)
                if s == 12:
                    pe.wait_ge(state_done, t + 1)
                    if not isinstance(t, int) or t:
                        pe.wait_ge(hn_done, t)
                    nc.tensor.matmul(ps_hn[:, :], w_t[:, W_HN, :], state[:, :],
                                     start=True, stop=True).then_inc(hn_mm, 1)
                if s == 13:
                    if not isinstance(t, int) or t:
                        pe.wait_ge(r_done, t)
                    nc.tensor.matmul(ps_r[:, :], w_t[:, W_HR, :], state[:, :], start=True, stop=False)
                if s == 14:
                    if not isinstance(t, int) or t:
                        pe.wait_ge(z_done, t)
                    nc.tensor.matmul(ps_z[:, :], w_t[:, W_HZ, :], state[:, :], start=True, stop=False)

            def gru(u, s):
                if s == 2:
                    pe.wait_ge(agg_done, u + 1)
                    if not isinstance(u, int) or u:
                        pe.wait_ge(normed, PER * u)
                    nc.tensor.matmul(ps_m[:, :], w_t[:, W_MSG, :], agg[:, :], start=True, stop=True).then_inc(msg_mm, 1)
                if s == 4:
                    pe.wait_ge(msg_done, u + 1)
                    nc.tensor.matmul(ps_r[:, :], w_t[:, W_IR, :], msg[:, :], start=False, stop=True).then_inc(r_mm, 1)
                if s == 5:
                    nc.tensor.matmul(ps_z[:, :], w_t[:, W_IZ, :], msg[:, :], start=False, stop=True).then_inc(z_mm, 1)
                if s == 6:
                    if not isinstance(u, int) or u:
                        pe.wait_ge(cand_in, u)
                    nc.tensor.matmul(ps_in[:, :], w_t[:, W_IN, :], msg[:, :], start=True, stop=True).then_inc(n_mm, 1)
                if s == 11:
                    pe.wait_ge(total_done, u + 1)
                    for b in range(PER):
                        last = nc.tensor.transpose(ps_m[:, b * P:(b + 1) * P], mixed[:, b * P:(b + 1) * P], ident[:, :])
                    last.then_inc(sum_turned, 1)

            pe.wait_ge(ident_done, 2)
            pe.wait_ge(w_in, 16 * 6)
            for k in range(7):
                dst = ps_h[:, k * D:(k + 1) * D] if k < 4 else ps_m[:, (k - 4) * D:(k - 3) * D]
                last = nc.tensor.transpose(dst, w_rows[:, k, :], ident[:, :])
            nc.tensor.transpose(ps_m[:, 3 * D:3 * D + 7], bias_rows[:, :], ident[0:7, 0:7]).then_inc(w_turned, 1)
            for s in range(PIECES):
                products(0, s, True)
                if s:
                    low_products(0, s - 1)
                if s == 8:
                    pe.wait_ge(w_done, 3)
                early(0, s)
            with pe.Fori(1, TILES) as t:
                for s in range(PIECES):
                    products(t, s, False)
                    low_products(t - 1, PIECES - 1) if s == 0 else low_products(t, s - 1)
                    gru(t - 1, s)
                    early(t, s)
            low_products(TILES - 1, PIECES - 1)
            for s in range(PIECES):
                gru(TILES - 1, s)


_INS = ["x", "adj", "L0_gnn_W_msg", "L0_gnn_b_msg", "L0_gnn_W_ih", "L0_gnn_W_hh", "L0_gnn_b_ih", "L0_gnn_b_hh"]


def kernel(**inputs):
    import numpy as _np
    import concourse.bacc as _bacc
    from concourse import mybir as _mybir
    from concourse.bass_utils import run_bass_kernel_spmd as _run

    nc = _bacc.Bacc("TRN2", target_bir_lowering=False, num_devices=1)
    arrays, args = {}, []
    for name in _INS:
        a = _np.ascontiguousarray(inputs[name])
        arrays[f"in_{name}"] = a
        args.append(nc.dram_tensor(f"in_{name}", a.shape, _mybir.dt.from_np(a.dtype), kind="ExternalInput").ap())
    out = nc.dram_tensor("out", inputs["x"].shape, _mybir.dt.float32, kind="ExternalOutput").ap()
    gated_graph_layer(nc, *args, out)
    r = _run(nc, [arrays], core_ids=[0])
    return r.results[0]["out"]
```

```python
import concourse.bass as bass
from concourse import mybir
from contextlib import ExitStack


def gated_graph_layer(nc, x, adj, w_msg, b_msg, w_ih, w_hh, b_ih, b_hh, out):
    fp32 = mybir.dt.float32
    f32r = mybir.dt.float32r
    ALU = mybir.AluOpType
    ACT = mybir.ActivationFunctionType

    LANES = 32
    P = 128
    QUADS = P // LANES
    N, D = x.shape
    SPAN = N // QUADS
    BLOCKS = SPAN // LANES
    PER = 4
    SPLIT = PER - 1
    TILES = BLOCKS // PER
    ROWS = PER * P
    GROUPS = ROWS // LANES
    CHUNKS = 4
    PIECES = BLOCKS // PER
    PIECES_CHUNK = PIECES // CHUNKS
    COLS = PIECES_CHUNK * PER * LANES
    RAW = 2
    RING = 4
    HALVES = 2
    CHUNK_INC = 16 * GROUPS
    EPS = 1e-5
    VE_LOW = (1, 3)
    VE_TILE = len(VE_LOW) * CHUNKS
    LAG = 2

    adj_v = adj.rearrange("(g t b c) (h j) -> g b t h c j", g=QUADS, t=TILES, b=PER, h=QUADS)
    x_v = x.rearrange("(h b c) d -> h c b d", h=QUADS, c=LANES)
    out_v = out.rearrange("(h t p) d -> t p h d", h=QUADS, t=TILES)

    def by_vector(s):
        return s % PIECES_CHUNK in VE_LOW

    def ve_lows(s):
        return sum(by_vector(k) for k in range(s)) if s >= 0 else ve_lows(s + PIECES) - VE_TILE

    ctx = ExitStack()
    with ctx:
        def sb(name, shape, dt=fp32):
            return ctx.enter_context(nc.sbuf_tensor(name, shape, dt))

        def bank(name):
            return ctx.enter_context(nc.psum_tensor(name, [P, ROWS], fp32))

        def sem(name):
            return ctx.enter_context(nc.semaphore(name))

        raw = sb("raw", [P, RAW, GROUPS, COLS])
        turned = sb("turned", [P, RING, PER, ROWS])
        high = sb("high", [P, HALVES, SPLIT * ROWS], f32r)
        low = sb("low", [P, HALVES, SPLIT * ROWS], f32r)
        x_high = sb("x_high", [P, TILES, SPLIT * D], f32r)
        x_low = sb("x_low", [P, TILES, SPLIT * D], f32r)
        x_whole = sb("x_whole", [P, TILES, D])
        work = sb("work", [P, 4, ROWS])
        x_stage = work[:, :, :]
        agg, mixed, half_hn, y_flat = (work[:, k, :] for k in range(4))
        tanh_z = half_hn
        y = y_flat.rearrange("p (h d) -> p h d", d=D)
        sum_a = sb("sum_a", [P, ROWS])
        msg_high = sb("msg_high", [P, ROWS], f32r)
        msg_low = sb("msg_low", [P, ROWS], f32r)
        state_high = sb("state_high", [P, ROWS], f32r)
        state_low = sb("state_low", [P, ROWS], f32r)
        rows_high = sb("rows_high", [P, SPLIT * D], f32r)
        rows_low = sb("rows_low", [P, SPLIT * D], f32r)
        rows_whole = sb("rows_whole", [P, D])
        stats = sb("stats", [P, QUADS, 6])
        moments = sb("moments", [P, QUADS, 2])
        rstd = sb("rstd", [P, QUADS])
        var_eps = sb("var_eps", [P, QUADS])
        eps = sb("eps", [P, QUADS])
        waited = sb("waited", [P, 1])
        zero = sb("zero", [P, QUADS])
        minus_mean = sb("minus_mean", [P, QUADS])
        shift = sb("shift", [P, QUADS])
        minus_half = sb("minus_half", [P, QUADS])
        staged = turned[:, RING - 1, :, :].rearrange("p b (k d) -> p (b k) d", d=D)
        w_rows = staged[:, 0:7, :]
        bias_rows = staged[0:7, 7, :]
        w_msg_t = sb("w_msg_t", [P, D])
        w_high = sb("w_high", [P, 6, D], f32r)
        w_low = sb("w_low", [P, 6, D], f32r)
        ident = sb("ident", [P, P])
        ident_r = sb("ident_r", [P, P], f32r)
        bias = sb("bias", [P, 7])
        half_bias = sb("half_bias", [P, 3])

        ps_a = bank("ps_a")
        ps_b = bank("ps_b")
        ps_m = bank("ps_m")
        ps_h = bank("ps_h")
        ps_r = bank("ps_r")
        ps_z = bank("ps_z")
        ps_n = bank("ps_n")
        ps_high = bank("ps_high")

        W_IR, W_IZ, W_IN, W_HR, W_HZ, W_HN = range(6)
        B_MSG, B_IR, B_IZ, B_IN, B_HR, B_HZ, B_HN = range(7)

        raw_in = [sem(f"raw_in{k}") for k in range(RAW)]
        x_in = sem("x_in")
        w_in = sem("w_in")
        x_high_done = sem("x_high_done")
        x_low_done = sem("x_low_done")
        piece_turned = sem("piece_turned")
        high_done = sem("high_done")
        low_done = sem("low_done")
        high_copied = sem("high_copied")
        ve_low_done = sem("ve_low_done")
        high_used = sem("high_used")
        piece_used = sem("piece_used")
        ident_done = sem("ident_done")
        identity_done = sem("identity_done")
        consts_done = sem("consts_done")
        w_turned = sem("w_turned")
        w_done = sem("w_done")
        w_high_done = sem("w_high_done")
        w_low_done = sem("w_low_done")
        bias_done = sem("bias_done")
        a_copied = sem("a_copied")
        agg_done = sem("agg_done")
        rows_done = sem("rows_done")
        state_turned = sem("state_turned")
        state_high_done = sem("state_high_done")
        state_done = sem("state_done")
        msg_mm = sem("msg_mm")
        relu_done = sem("relu_done")
        msg_high_done = sem("msg_high_done")
        msg_done = sem("msg_done")
        r_mm = sem("r_mm")
        z_mm = sem("z_mm")
        n_mm = sem("n_mm")
        hn_done = sem("hn_done")
        r_done = sem("r_done")
        z_done = sem("z_done")
        gated = sem("gated")
        cand_in = sem("cand_in")
        cand_done = sem("cand_done")
        state_scaled = sem("state_scaled")
        cand_scaled = sem("cand_scaled")
        hn_mm = sem("hn_mm")
        total_done = sem("total_done")
        sum_turned = sem("sum_turned")
        stats_done = sem("stats_done")
        moments_done = sem("moments_done")
        var_done = sem("var_done")
        rstd_done = sem("rstd_done")
        mean_done = sem("mean_done")
        shift_done = sem("shift_done")
        normed = sem("normed")
        stored = sem("stored")

        block = ctx.enter_context(nc.Block())

        @block.sync
        def _(sp):
            def load_x(q):
                if q:
                    sp.wait_ge(x_high_done, 2 * q)
                    sp.wait_ge(x_low_done, q)
                lo = q * BLOCKS // CHUNKS
                for h in range(QUADS):
                    sp.dma_start(x_stage[LANES * h:LANES * (h + 1), :, :].rearrange("p k (b d) -> p (k b) d", d=D),
                                 x_v[h, :, lo:lo + BLOCKS // CHUNKS, :]).then_inc(x_in, 16)

            def load_chunk(t, q):
                slot = q % RAW
                for g in range(GROUPS):
                    quad, b = divmod(g, PER)
                    sp.dma_start(raw[:, slot, g, :],
                                 adj_v[quad, b, t, :, :, q * COLS:(q + 1) * COLS]).then_inc(raw_in[slot], 16)

            def next_chunk(t, q):
                sp.wait_ge(piece_turned, PIECES * t + PIECES_CHUNK * (q - RAW + 1))
                load_chunk(t, q)

            def store(u):
                sp.wait_ge(normed, QUADS * (u + 1))
                sp.dma_start(out_v[u], y).then_inc(stored, 16)

            def store_quad(u, h):
                sp.wait_ge(normed, QUADS * u + h + 1)
                sp.dma_start(out_v[u, :, h], y[:, h, :]).then_inc(stored, 16)

            for q in range(CHUNKS):
                load_x(q)
                if q >= RAW:
                    sp.wait_ge(piece_turned, PIECES_CHUNK * (q - RAW + 1))
                load_chunk(0, q)
            for q in range(CHUNKS):
                next_chunk(1, q)
            with sp.Fori(2, TILES) as t:
                for q in range(CHUNKS):
                    if q == 2:
                        store(t - 2)
                    next_chunk(t, q)
            store(TILES - 2)
            for h in range(QUADS):
                store_quad(TILES - 1, h)
            sp.wait_ge(stored, 16 * (TILES - 1 + QUADS))

        @block.vector
        def _(ve):
            def split_x(q):
                ve.wait_ge(x_high_done, 2 * q + 1)
                stage = x_stage.rearrange("p k (b d) -> p k (b d)", d=D)[:, :, 0:SPLIT * D]
                ts = slice(q * TILES // CHUNKS, (q + 1) * TILES // CHUNKS)
                nc.vector.tensor_tensor(x_low[:, ts, :], stage, x_high[:, ts, :].bitcast(fp32),
                                        ALU.subtract).then_inc(x_low_done, 1)

            def turn(t, s, first):
                q, k = divmod(s, PIECES_CHUNK)
                if k == 0:
                    ve.wait_ge(raw_in[q % RAW], CHUNK_INC * (CHUNKS // RAW * t + q // RAW + 1))
                if first and s == RING - 1:
                    ve.wait_ge(w_turned, 1)
                if not first or s >= RING:
                    ve.wait_ge(high_used, PIECES * t + s - RING + 1)
                    ve.wait_ge(low_done, PIECES * t + s - RING + 1)
                    if by_vector(s - RING):
                        ve.wait_ge(ve_low_done, VE_TILE * t + ve_lows(s - RING + 1))
                src = raw[:, q % RAW, :, k * PER * LANES:(k + 1) * PER * LANES]
                dst = turned[:, s % RING, :, :].rearrange("p b (g c) -> p g b c", c=LANES)
                nc.vector.transpose(dst, src).then_inc(piece_turned, 1)

            def subtract_low(t, s, first):
                ve.wait_ge(high_copied, VE_TILE * t + ve_lows(s) + 1)
                if not first or s >= HALVES:
                    ve.wait_ge(piece_used, PIECES * t + s - HALVES + 1)
                nc.vector.tensor_tensor(low[:, s % HALVES, (SPLIT - 1) * ROWS:], turned[:, s % RING, SPLIT - 1, :],
                                        ps_high[:, :], ALU.subtract).then_inc(ve_low_done, 1)

            def lows(t, s, first):
                if s >= LAG:
                    if by_vector(s - LAG):
                        subtract_low(t, s - LAG, first)
                elif not first and by_vector(PIECES + s - LAG):
                    subtract_low(t - 1, PIECES + s - LAG, False)

            def early(t, s):
                if s == 15:
                    ve.wait_ge(state_high_done, t + 1)
                    nc.vector.tensor_tensor(state_low[:, :], ps_h[:, :], state_high[:, :].bitcast(fp32),
                                            ALU.subtract).then_inc(state_done, 1)

            def gru(u, s):
                if s == 3:
                    ve.wait_ge(piece_used, PIECES * (u + 1))
                    ve.wait_ge(a_copied, u + 1)
                    nc.vector.tensor_tensor(agg, ps_b[:, :], sum_a[:, :], ALU.add).then_inc(agg_done, 1)
                if s == 6:
                    ve.wait_ge(msg_high_done, u + 1)
                    nc.vector.tensor_tensor(msg_low[:, :], ps_m[:, :], msg_high[:, :].bitcast(fp32),
                                            ALU.subtract).then_inc(msg_done, 1)
                if s == 9:
                    ve.wait_ge(r_done, u + 1)
                    nc.vector.scalar_tensor_tensor(mixed, ps_r[:, :], 1.0, half_hn,
                                                   ALU.add, ALU.mult).then_inc(gated, 1)
                if s == 10:
                    ve.wait_ge(gated, u + 1)
                    ve.wait_ge(n_mm, u + 1)
                    nc.vector.tensor_tensor(mixed, ps_n[:, :], mixed, ALU.add).then_inc(cand_in, 1)
                if s == 11:
                    ve.wait_ge(z_done, u + 1)
                    nc.vector.scalar_tensor_tensor(ps_h[:, :], tanh_z, 3.0, ps_h[:, :],
                                                   ALU.add, ALU.mult).then_inc(state_scaled, 1)
                    ve.wait_ge(cand_done, u + 1)
                    nc.vector.scalar_tensor_tensor(mixed, tanh_z, 1.0, ps_n[:, :],
                                                   ALU.subtract, ALU.mult).then_inc(cand_scaled, 1)
                    ve.wait_ge(state_scaled, u + 1)
                    ve.wait_ge(cand_scaled, u + 1)
                    nc.vector.tensor_tensor(mixed, ps_h[:, :], mixed, ALU.subtract).then_inc(total_done, 1)
                if s == 14:
                    ve.wait_ge(sum_turned, u + 1)
                    for h in range(QUADS):
                        nc.vector.bn_stats(stats[:, h, :], ps_m[:, h * D:(h + 1) * D]).then_inc(stats_done, 1)
                    ve.wait_ge(stats_done, QUADS * (u + 1))
                    nc.vector.tensor_copy(waited[:, :], eps[:, 0:1])
                    for h in range(QUADS):
                        nc.vector.bn_aggr(moments[:, h, :], stats[:, h, :]).then_inc(moments_done, 1)

            nc.vector.memset(zero[:, :], 0.0).then_inc(consts_done, 1)
            nc.vector.memset(eps[:, :], 4 * EPS).then_inc(consts_done, 1)
            nc.vector.memset(minus_half[:, :], -0.5).then_inc(consts_done, 1)
            split_x(0)
            ve.wait_ge(w_done, 2)
            nc.vector.tensor_tensor(half_bias[:, 0:2], bias[:, B_IR:B_IR + 2], bias[:, B_HR:B_HR + 2],
                                    ALU.add).then_inc(bias_done, 1)
            nc.vector.tensor_copy(half_bias[:, 2:3], bias[:, B_HN:B_HN + 1]).then_inc(bias_done, 1)
            ve.wait_ge(w_high_done, 2)
            nc.vector.tensor_tensor(w_low[:, 0:3, :], ps_h[:, D:4 * D].rearrange("p (k d) -> p k d", d=D),
                                    w_high[:, 0:3, :].bitcast(fp32), ALU.subtract).then_inc(w_low_done, 1)
            nc.vector.tensor_tensor(w_low[:, 3:6, :], ps_m[:, 0:3 * D].rearrange("p (k d) -> p k d", d=D),
                                    w_high[:, 3:6, :].bitcast(fp32), ALU.subtract).then_inc(w_low_done, 1)
            ve.wait_ge(bias_done, 2)
            nc.vector.tensor_scalar(half_bias[:, :], half_bias[:, :], 0.5, None,
                                    ALU.mult).then_inc(bias_done, 1)
            for s in range(PIECES):
                turn(0, s, True)
                lows(0, s, True)
                if s % PIECES_CHUNK == PIECES_CHUNK - 1 and s // PIECES_CHUNK < CHUNKS - 1:
                    split_x(s // PIECES_CHUNK + 1)
                early(0, s)
            with ve.Fori(1, TILES) as t:
                for s in range(PIECES):
                    turn(t, s, False)
                    lows(t, s, False)
                    gru(t - 1, s)
                    early(t, s)
            for s in range(PIECES - LAG, PIECES):
                if by_vector(s):
                    subtract_low(TILES - 1, s, False)
            for s in range(PIECES):
                gru(TILES - 1, s)

        @block.scalar
        def _(act):
            act.dma_start(w_rows[:, 0, :], w_msg).then_inc(w_in, 16)
            act.dma_start(w_rows[:, 1:4, :], w_ih.rearrange("(k e) d -> e k d", e=P)).then_inc(w_in, 16)
            act.dma_start(w_rows[:, 4:7, :], w_hh.rearrange("(k e) d -> e k d", e=P)).then_inc(w_in, 16)
            act.dma_start(bias_rows[0:1, :], b_msg.rearrange("(k e) -> k e", k=1)).then_inc(w_in, 16)
            act.dma_start(bias_rows[1:4, :], b_ih.rearrange("(k e) -> k e", e=P)).then_inc(w_in, 16)
            act.dma_start(bias_rows[4:7, :], b_hh.rearrange("(k e) -> k e", e=P)).then_inc(w_in, 16)

            def split_x(q):
                act.wait_ge(x_in, 16 * QUADS * (q + 1))
                ts = slice(q * TILES // CHUNKS, (q + 1) * TILES // CHUNKS)
                nc.scalar.activation(x_high[:, ts, :], x_stage[:, :, 0:SPLIT * D], ACT.Copy).then_inc(x_high_done, 1)
                nc.scalar.activation(x_whole[:, ts, :], x_stage[:, :, SPLIT * D:], ACT.Copy).then_inc(x_high_done, 1)

            def round_high(t, s, first):
                act.wait_ge(piece_turned, PIECES * t + s + 1)
                if not first or s >= HALVES:
                    act.wait_ge(high_used, PIECES * t + s - HALVES + 1)
                    act.wait_ge(low_done, PIECES * t + s - HALVES + 1)
                    if by_vector(s - HALVES):
                        act.wait_ge(high_copied, VE_TILE * t + ve_lows(s - HALVES + 1))
                nc.scalar.activation(high[:, s % HALVES, :],
                                     turned[:, s % RING, 0:SPLIT, :].rearrange("p b r -> p (b r)"),
                                     ACT.Copy).then_inc(high_done, 1)
                if by_vector(s):
                    act.wait_ge(high_done, PIECES * t + s + 1)
                    if not first or ve_lows(s):
                        act.wait_ge(ve_low_done, VE_TILE * t + ve_lows(s))
                    nc.scalar.activation(ps_high[:, :], high[:, s % HALVES, (SPLIT - 1) * ROWS:].bitcast(fp32),
                                         ACT.Copy).then_inc(high_copied, 1)

            def early(t, s):
                if s == 8:
                    if not isinstance(t, int) or t:
                        act.wait_ge(state_turned, t)
                    one = bass.ds(t, 1)
                    for rows, held in ((rows_high, x_high), (rows_low, x_low), (rows_whole, x_whole)):
                        nc.scalar.activation(rows[:, :].rearrange("p (o n) -> p o n", o=1),
                                             held[:, one, :].bitcast(fp32), ACT.Copy).then_inc(rows_done, 1)
                if s == 13:
                    act.wait_ge(state_turned, t + 1)
                    nc.scalar.activation(state_high[:, :], ps_h[:, :], ACT.Copy).then_inc(state_high_done, 1)

            def gru(u, s):
                if s == 2:
                    act.wait_ge(hn_mm, u + 1)
                    if not isinstance(u, int) or u:
                        act.wait_ge(cand_scaled, u)
                    nc.scalar.activation(half_hn, ps_n[:, :], ACT.Identity, bias=half_bias[:, 2:3],
                                         scale=0.5).then_inc(hn_done, 1)
                if s == 4:
                    act.wait_ge(msg_mm, u + 1)
                    nc.scalar.activation(ps_m[:, :], ps_m[:, :], ACT.Relu,
                                         bias=bias[:, B_MSG:B_MSG + 1]).then_inc(relu_done, 1)
                    act.wait_ge(relu_done, u + 1)
                    nc.scalar.activation(msg_high[:, :], ps_m[:, :], ACT.Copy).then_inc(msg_high_done, 1)
                if s == 7:
                    act.wait_ge(r_mm, u + 1)
                    nc.scalar.activation(ps_r[:, :], ps_r[:, :], ACT.Tanh, bias=half_bias[:, 0:1],
                                         scale=0.5).then_inc(r_done, 1)
                if s == 9:
                    act.wait_ge(z_mm, u + 1)
                    act.wait_ge(gated, u + 1)
                    nc.scalar.activation(tanh_z, ps_z[:, :], ACT.Tanh, bias=half_bias[:, 1:2],
                                         scale=0.5).then_inc(z_done, 1)
                    act.wait_ge(cand_in, u + 1)
                    nc.scalar.activation(ps_n[:, :], mixed, ACT.Tanh,
                                         bias=bias[:, B_IN:B_IN + 1]).then_inc(cand_done, 1)
                if s == 15:
                    act.wait_ge(shift_done, u + 1)
                    if not isinstance(u, int) or u:
                        act.wait_ge(stored, 16 * u)
                    for h in range(QUADS):
                        nc.scalar.activation(y[:, h, :], ps_m[:, h * D:(h + 1) * D], ACT.Identity,
                                             bias=shift[:, h:h + 1], scale=rstd[:, h:h + 1]).then_inc(normed, 1)

            def copy_a(t, s):
                if s == PIECES // 2 + 2:
                    act.wait_ge(piece_used, PIECES * t + PIECES // 2)
                    if not isinstance(t, int) or t:
                        act.wait_ge(agg_done, t)
                    nc.scalar.activation(sum_a[:, :], ps_a[:, :], ACT.Copy).then_inc(a_copied, 1)

            split_x(0)
            act.wait_ge(w_turned, 1)
            nc.scalar.activation(w_high[:, 0:3, :].rearrange("p k d -> p (k d)"), ps_h[:, D:4 * D],
                                 ACT.Copy).then_inc(w_high_done, 1)
            nc.scalar.activation(w_high[:, 3:6, :].rearrange("p k d -> p (k d)"), ps_m[:, 0:3 * D],
                                 ACT.Copy).then_inc(w_high_done, 1)
            nc.scalar.activation(w_msg_t[:, :], ps_h[:, 0:D], ACT.Copy).then_inc(w_done, 1)
            nc.scalar.activation(bias[:, :], ps_m[:, 3 * D:3 * D + 7], ACT.Copy).then_inc(w_done, 1)
            act.wait_ge(ident_done, 2)
            nc.scalar.activation(ident_r[:, :], ident[:, :], ACT.Copy).then_inc(identity_done, 1)
            for s in range(PIECES):
                round_high(0, s, True)
                copy_a(0, s)
                early(0, s)
                if s == PIECES - 1:
                    act.wait_ge(bias_done, 3)
                if s % PIECES_CHUNK == 1 and s // PIECES_CHUNK < CHUNKS - 1:
                    split_x(s // PIECES_CHUNK + 1)
            with act.Fori(1, TILES) as t:
                for s in range(PIECES):
                    round_high(t, s, False)
                    copy_a(t, s)
                    gru(t - 1, s)
                    early(t, s)
            for s in range(PIECES):
                gru(TILES - 1, s)

        @block.gpsimd
        def _(pool):
            nc.gpsimd.memset(ident[:, :], 0.0).then_inc(ident_done, 1)
            pool.wait_ge(ident_done, 1)
            nc.gpsimd.affine_select(out=ident[:, :], in_=ident[:, :], compare_op=ALU.not_equal, fill=1.0, base=0,
                                    pattern=[[-1, P]], channel_multiplier=1).then_inc(ident_done, 1)

            def subtract_low(t, s, first):
                pool.wait_ge(high_done, PIECES * t + s + 1)
                if not first or s >= HALVES:
                    pool.wait_ge(piece_used, PIECES * t + s - HALVES + 1)
                n = (SPLIT - by_vector(s)) * ROWS
                nc.gpsimd.tensor_tensor(low[:, s % HALVES, 0:n],
                                        turned[:, s % RING, :, :].rearrange("p b r -> p (b r)")[:, 0:n],
                                        high[:, s % HALVES, 0:n].bitcast(fp32),
                                        ALU.subtract).then_inc(low_done, 1)

            def gru(u, s):
                if s == 13:
                    pool.wait_ge(moments_done, QUADS * (u + 1))
                    if not isinstance(u, int) or u:
                        pool.wait_ge(normed, QUADS * u)
                    nc.gpsimd.tensor_tensor(var_eps[:, :], moments[:, :, 1], eps[:, :],
                                            ALU.add).then_inc(var_done, 1)
                    pool.wait_ge(var_done, u + 1)
                    nc.gpsimd.tensor_tensor(rstd[:, :], var_eps[:, :], minus_half[:, :],
                                            ALU.pow).then_inc(rstd_done, 1)
                    pool.wait_ge(rstd_done, u + 1)
                    nc.gpsimd.tensor_tensor(minus_mean[:, :], zero[:, :], moments[:, :, 0],
                                            ALU.subtract).then_inc(mean_done, 1)
                    pool.wait_ge(mean_done, u + 1)
                    nc.gpsimd.tensor_tensor(shift[:, :], minus_mean[:, :], rstd[:, :],
                                            ALU.mult).then_inc(shift_done, 1)

            pool.wait_ge(consts_done, 3)
            for s in range(PIECES):
                subtract_low(0, s, True)
            with pool.Fori(1, TILES) as t:
                for s in range(PIECES):
                    subtract_low(t, s, False)
                    gru(t - 1, s)
            for s in range(PIECES):
                gru(TILES - 1, s)

        @block.tensor
        def _(pe):
            def products(t, s, first):
                ps = ps_a if s < PIECES // 2 else ps_b
                if s % (PIECES // 2) == 0 and not first:
                    if s == 0:
                        pe.wait_ge(a_copied, t)
                    else:
                        pe.wait_ge(agg_done, t)
                if first and s % PIECES_CHUNK == 0:
                    pe.wait_ge(x_high_done, 2 * (s // PIECES_CHUNK + 1))
                    pe.wait_ge(x_low_done, s // PIECES_CHUNK + 1)
                pe.wait_ge(piece_turned, PIECES * t + s + 1)
                nc.tensor.matmul(ps[:, :], x_whole[:, s, :], turned[:, s % RING, SPLIT, :],
                                 start=(s % (PIECES // 2) == 0), stop=False)
                pe.wait_ge(high_done, PIECES * t + s + 1)
                for b in range(SPLIT):
                    rhs = high[:, s % HALVES, b * ROWS:(b + 1) * ROWS]
                    nc.tensor.matmul(ps[:, :], x_low[:, s, b * D:(b + 1) * D], rhs, start=False, stop=False)
                    last = nc.tensor.matmul(ps[:, :], x_high[:, s, b * D:(b + 1) * D], rhs, start=False, stop=False)
                last.then_inc(high_used, 1)

            def low_products(t, s):
                ps = ps_a if s < PIECES // 2 else ps_b
                stop = s % (PIECES // 2) == PIECES // 2 - 1
                pe.wait_ge(low_done, PIECES * t + s + 1)
                if by_vector(s):
                    pe.wait_ge(ve_low_done, VE_TILE * t + ve_lows(s) + 1)
                for b in range(SPLIT):
                    last = nc.tensor.matmul(ps[:, :], x_high[:, s, b * D:(b + 1) * D],
                                            low[:, s % HALVES, b * ROWS:(b + 1) * ROWS],
                                            start=False, stop=stop and b == SPLIT - 1)
                last.then_inc(piece_used, 1)

            def in_halves(ps, w, high_half, low_half, start, stop):
                nc.tensor.matmul(ps[:, :], w_low[:, w, :], high_half[:, :], start=start, stop=False)
                nc.tensor.matmul(ps[:, :], w_high[:, w, :], low_half[:, :], start=False, stop=False)
                return nc.tensor.matmul(ps[:, :], w_high[:, w, :], high_half[:, :], start=False, stop=stop)

            def early(t, s):
                if s == 10:
                    pe.wait_ge(rows_done, 3 * (t + 1))
                    if not isinstance(t, int) or t:
                        pe.wait_ge(state_done, t)
                        pe.wait_ge(total_done, t)
                    state = ps_h[:, :].rearrange("p (h b c) -> p b h c", h=QUADS, b=PER)
                    for b in range(SPLIT):
                        rows = slice(b * D, (b + 1) * D)
                        nc.tensor.matmul(state[:, b], rows_high[:, rows], ident_r[:, :], start=True, stop=False)
                        nc.tensor.matmul(state[:, b], rows_low[:, rows], ident_r[:, :], start=False, stop=True)
                    nc.tensor.transpose(state[:, SPLIT], rows_whole[:, :], ident[:, :]).then_inc(state_turned, 1)
                if s == 14:
                    pe.wait_ge(state_done, t + 1)
                    if not isinstance(t, int) or t:
                        pe.wait_ge(gated, t)
                    in_halves(ps_r, W_HR, state_high, state_low, True, False)
                if s == 15:
                    if not isinstance(t, int) or t:
                        pe.wait_ge(z_done, t)
                    in_halves(ps_z, W_HZ, state_high, state_low, True, False)

            def gru(u, s):
                if s == 0:
                    if not isinstance(u, int) or u:
                        pe.wait_ge(cand_scaled, u)
                    in_halves(ps_n, W_HN, state_high, state_low, True, True).then_inc(hn_mm, 1)
                if s == 2:
                    pe.wait_ge(agg_done, u + 1)
                    if not isinstance(u, int) or u:
                        pe.wait_ge(normed, QUADS * u)
                    nc.tensor.matmul(ps_m[:, :], w_msg_t[:, :], agg, start=True, stop=True).then_inc(msg_mm, 1)
                if s == 5:
                    pe.wait_ge(msg_done, u + 1)
                    in_halves(ps_r, W_IR, msg_high, msg_low, False, True).then_inc(r_mm, 1)
                if s == 6:
                    in_halves(ps_z, W_IZ, msg_high, msg_low, False, True).then_inc(z_mm, 1)
                    pe.wait_ge(hn_done, u + 1)
                    in_halves(ps_n, W_IN, msg_high, msg_low, True, True).then_inc(n_mm, 1)
                if s == 11:
                    pe.wait_ge(total_done, u + 1)
                    for h in range(QUADS):
                        cols = slice(h * P, (h + 1) * P)
                        last = nc.tensor.transpose(ps_m[:, cols], mixed[:, cols], ident[:, :])
                    last.then_inc(sum_turned, 1)

            pe.wait_ge(ident_done, 2)
            pe.wait_ge(w_in, 16 * 6)
            for k in range(7):
                dst = ps_h[:, k * D:(k + 1) * D] if k < 4 else ps_m[:, (k - 4) * D:(k - 3) * D]
                last = nc.tensor.transpose(dst, w_rows[:, k, :], ident[:, :])
            nc.tensor.transpose(ps_m[:, 3 * D:3 * D + 7], bias_rows, ident[0:7, 0:7]).then_inc(w_turned, 1)
            for s in range(PIECES):
                products(0, s, True)
                if s:
                    low_products(0, s - 1)
                if s == 8:
                    pe.wait_ge(w_done, 2)
                    pe.wait_ge(w_high_done, 2)
                    pe.wait_ge(identity_done, 1)
                    pe.wait_ge(w_low_done, 2)
                early(0, s)
            with pe.Fori(1, TILES) as t:
                for s in range(PIECES):
                    products(t, s, False)
                    low_products(t - 1, PIECES - 1) if s == 0 else low_products(t, s - 1)
                    gru(t - 1, s)
                    early(t, s)
            low_products(TILES - 1, PIECES - 1)
            for s in range(PIECES):
                gru(TILES - 1, s)


_INS = ["x", "adj", "L0_gnn_W_msg", "L0_gnn_b_msg", "L0_gnn_W_ih", "L0_gnn_W_hh", "L0_gnn_b_ih", "L0_gnn_b_hh"]


def kernel(**inputs):
    import numpy as _np
    import concourse.bacc as _bacc
    from concourse import mybir as _mybir
    from concourse.bass_utils import run_bass_kernel_spmd as _run

    nc = _bacc.Bacc("TRN2", target_bir_lowering=False, num_devices=1)
    arrays, args = {}, []
    for name in _INS:
        a = _np.ascontiguousarray(inputs[name])
        arrays[f"in_{name}"] = a
        args.append(nc.dram_tensor(f"in_{name}", a.shape, _mybir.dt.from_np(a.dtype), kind="ExternalInput").ap())
    out = nc.dram_tensor("out", inputs["x"].shape, _mybir.dt.float32, kind="ExternalOutput").ap()
    gated_graph_layer(nc, *args, out)
    r = _run(nc, [arrays], core_ids=[0])
    return r.results[0]["out"]
```
